# Optimizing a Trainium2 kernel written in Bass

```python
import numpy as np
import jax
import jax.numpy as jnp

def _softmax(x, axis=-1):
    return jax.nn.softmax(x, axis=axis)

def _gelu(x):
    return jax.nn.gelu(x, approximate=True)

def _silu(x):
    return jax.nn.silu(x)

def _sigmoid(x):
    return jax.nn.sigmoid(x)

def _layernorm(x, axis=-1, eps=1e-05):
    m = jnp.mean(x, axis=axis, keepdims=True)
    v = jnp.var(x, axis=axis, keepdims=True)
    return (x - m) / jnp.sqrt(v + eps)

def _scatter_add(tgt, idx, src, axis=0):
    return tgt.at[idx].add(src)

def _segment_sum(src, seg, n):
    return jax.ops.segment_sum(src, seg, n)
kernel_name = 'mk_dlrm_tower_d1_rec_r8_cf8154'

def setup_inputs(seed: int=0):
    np.random.seed(seed)
    _w = jnp.asarray

    def _rec_inputs():
        import jax
        import jax.numpy as jnp
        _tk = jax.random.key(seed)
        dense_ctx = jax.random.normal(jax.random.fold_in(_tk, 190), (2048, 16), jnp.float32)
        ids = jnp.stack([jax.random.randint(jax.random.fold_in(_tk, 200 + f), (2048,), 0, v, jnp.int32) for f, v in enumerate([1250, 1250, 125000, 125000, 125000, 1250, 1000, 125000, 12500, 12500, 1000, 1250, 125000, 1250, 12500, 1250, 12500, 12500, 1000, 1000, 1250, 1000, 125000, 12500, 12500, 1250, 1250, 1000, 1250, 12500, 1000, 1250, 12500, 1000, 1250, 12500, 1000, 12500, 1250, 1250])], axis=1)
        tbl_0 = 0.05 * jax.random.normal(jax.random.fold_in(_tk, 500 + 0), (1250, 32), jnp.float32)
        tbl_1 = 0.05 * jax.random.normal(jax.random.fold_in(_tk, 500 + 1), (1250, 32), jnp.float32)
        tbl_2 = 0.05 * jax.random.normal(jax.random.fold_in(_tk, 500 + 2), (125000, 32), jnp.float32)
        tbl_3 = 0.05 * jax.random.normal(jax.random.fold_in(_tk, 500 + 3), (125000, 32), jnp.float32)
        tbl_4 = 0.05 * jax.random.normal(jax.random.fold_in(_tk, 500 + 4), (125000, 32), jnp.float32)
        tbl_5 = 0.05 * jax.random.normal(jax.random.fold_in(_tk, 500 + 5), (1250, 32), jnp.float32)
        tbl_6 = 0.05 * jax.random.normal(jax.random.fold_in(_tk, 500 + 6), (1000, 32), jnp.float32)
        tbl_7 = 0.05 * jax.random.normal(jax.random.fold_in(_tk, 500 + 7), (125000, 32), jnp.float32)
        tbl_8 = 0.05 * jax.random.normal(jax.random.fold_in(_tk, 500 + 8), (12500, 32), jnp.float32)
        tbl_9 = 0.05 * jax.random.normal(jax.random.fold_in(_tk, 500 + 9), (12500, 32), jnp.float32)
        tbl_10 = 0.05 * jax.random.normal(jax.random.fold_in(_tk, 500 + 10), (1000, 32), jnp.float32)
        tbl_11 = 0.05 * jax.random.normal(jax.random.fold_in(_tk, 500 + 11), (1250, 32), jnp.float32)
        tbl_12 = 0.05 * jax.random.normal(jax.random.fold_in(_tk, 500 + 12), (125000, 32), jnp.float32)
        tbl_13 = 0.05 * jax.random.normal(jax.random.fold_in(_tk, 500 + 13), (1250, 32), jnp.float32)
        tbl_14 = 0.05 * jax.random.normal(jax.random.fold_in(_tk, 500 + 14), (12500, 32), jnp.float32)
        tbl_15 = 0.05 * jax.random.normal(jax.random.fold_in(_tk, 500 + 15), (1250, 32), jnp.float32)
        tbl_16 = 0.05 * jax.random.normal(jax.random.fold_in(_tk, 500 + 16), (12500, 32), jnp.float32)
        tbl_17 = 0.05 * jax.random.normal(jax.random.fold_in(_tk, 500 + 17), (12500, 32), jnp.float32)
        tbl_18 = 0.05 * jax.random.normal(jax.random.fold_in(_tk, 500 + 18), (1000, 32), jnp.float32)
        tbl_19 = 0.05 * jax.random.normal(jax.random.fold_in(_tk, 500 + 19), (1000, 32), jnp.float32)
        tbl_20 = 0.05 * jax.random.normal(jax.random.fold_in(_tk, 500 + 20), (1250, 32), jnp.float32)
        tbl_21 = 0.05 * jax.random.normal(jax.random.fold_in(_tk, 500 + 21), (1000, 32), jnp.float32)
        tbl_22 = 0.05 * jax.random.normal(jax.random.fold_in(_tk, 500 + 22), (125000, 32), jnp.float32)
        tbl_23 = 0.05 * jax.random.normal(jax.random.fold_in(_tk, 500 + 23), (12500, 32), jnp.float32)
        tbl_24 = 0.05 * jax.random.normal(jax.random.fold_in(_tk, 500 + 24), (12500, 32), jnp.float32)
        tbl_25 = 0.05 * jax.random.normal(jax.random.fold_in(_tk, 500 + 25), (1250, 32), jnp.float32)
        tbl_26 = 0.05 * jax.random.normal(jax.random.fold_in(_tk, 500 + 26), (1250, 32), jnp.float32)
        tbl_27 = 0.05 * jax.random.normal(jax.random.fold_in(_tk, 500 + 27), (1000, 32), jnp.float32)
        tbl_28 = 0.05 * jax.random.normal(jax.random.fold_in(_tk, 500 + 28), (1250, 32), jnp.float32)
        tbl_29 = 0.05 * jax.random.normal(jax.random.fold_in(_tk, 500 + 29), (12500, 32), jnp.float32)
        tbl_30 = 0.05 * jax.random.normal(jax.random.fold_in(_tk, 500 + 30), (1000, 32), jnp.float32)
        tbl_31 = 0.05 * jax.random.normal(jax.random.fold_in(_tk, 500 + 31), (1250, 32), jnp.float32)
        tbl_32 = 0.05 * jax.random.normal(jax.random.fold_in(_tk, 500 + 32), (12500, 32), jnp.float32)
        tbl_33 = 0.05 * jax.random.normal(jax.random.fold_in(_tk, 500 + 33), (1000, 32), jnp.float32)
        tbl_34 = 0.05 * jax.random.normal(jax.random.fold_in(_tk, 500 + 34), (1250, 32), jnp.float32)
        tbl_35 = 0.05 * jax.random.normal(jax.random.fold_in(_tk, 500 + 35), (12500, 32), jnp.float32)
        tbl_36 = 0.05 * jax.random.normal(jax.random.fold_in(_tk, 500 + 36), (1000, 32), jnp.float32)
        tbl_37 = 0.05 * jax.random.normal(jax.random.fold_in(_tk, 500 + 37), (12500, 32), jnp.float32)
        tbl_38 = 0.05 * jax.random.normal(jax.random.fold_in(_tk, 500 + 38), (1250, 32), jnp.float32)
        tbl_39 = 0.05 * jax.random.normal(jax.random.fold_in(_tk, 500 + 39), (1250, 32), jnp.float32)
        _rk = jax.random.fold_in(_tk, 7)
        W_top1 = 0.0354441 * jax.random.normal(jax.random.fold_in(_tk, 801), (796, 512), jnp.float32)
        W_top2 = 0.0441942 * jax.random.normal(jax.random.fold_in(_tk, 802), (512, 256), jnp.float32)
        W_top3 = 0.0625 * jax.random.normal(jax.random.fold_in(_tk, 803), (256, 1), jnp.float32)
        b_top1 = jnp.zeros((512,), jnp.float32)
        b_top2 = jnp.zeros((256,), jnp.float32)
        return (dense_ctx, ids, tbl_0, tbl_1, tbl_2, tbl_3, tbl_4, tbl_5, tbl_6, tbl_7, tbl_8, tbl_9, tbl_10, tbl_11, tbl_12, tbl_13, tbl_14, tbl_15, tbl_16, tbl_17, tbl_18, tbl_19, tbl_20, tbl_21, tbl_22, tbl_23, tbl_24, tbl_25, tbl_26, tbl_27, tbl_28, tbl_29, tbl_30, tbl_31, tbl_32, tbl_33, tbl_34, tbl_35, tbl_36, tbl_37, tbl_38, tbl_39, W_top1, b_top1, W_top2, b_top2, W_top3)
    dense_ctx, ids, tbl_0, tbl_1, tbl_2, tbl_3, tbl_4, tbl_5, tbl_6, tbl_7, tbl_8, tbl_9, tbl_10, tbl_11, tbl_12, tbl_13, tbl_14, tbl_15, tbl_16, tbl_17, tbl_18, tbl_19, tbl_20, tbl_21, tbl_22, tbl_23, tbl_24, tbl_25, tbl_26, tbl_27, tbl_28, tbl_29, tbl_30, tbl_31, tbl_32, tbl_33, tbl_34, tbl_35, tbl_36, tbl_37, tbl_38, tbl_39, W_top1, b_top1, W_top2, b_top2, W_top3 = _rec_inputs()

    def _L0_rec_setup():
        import jax, jax.numpy as jnp
        import numpy as np
        NUM_FIELDS = 40
        EMBED_DIM = 32
        BATCH = 512
        NUM_PAIRS = NUM_FIELDS * (NUM_FIELDS - 1) // 2
        key = jax.random.key(seed)
        k1, k2 = jax.random.split(key)
        inputs = jax.random.normal(k1, (BATCH, NUM_FIELDS, EMBED_DIM), dtype=jnp.float32)
        std = (2.0 / (EMBED_DIM + EMBED_DIM)) ** 0.5
        bilinear_matrices = jax.random.normal(k2, (NUM_PAIRS, EMBED_DIM, EMBED_DIM), dtype=jnp.float32) * std
        return {'inputs': inputs, 'bilinear_matrices': bilinear_matrices}
    _L0_rec_all = _L0_rec_setup()
    _L0_rec_in = {k: v for k, v in _L0_rec_all.items() if k in ('bilinear_matrices',)}
    del _L0_rec_all
    return {'dense_ctx': dense_ctx, 'ids': ids, 'tbl_0': tbl_0, 'tbl_1': tbl_1, 'tbl_2': tbl_2, 'tbl_3': tbl_3, 'tbl_4': tbl_4, 'tbl_5': tbl_5, 'tbl_6': tbl_6, 'tbl_7': tbl_7, 'tbl_8': tbl_8, 'tbl_9': tbl_9, 'tbl_10': tbl_10, 'tbl_11': tbl_11, 'tbl_12': tbl_12, 'tbl_13': tbl_13, 'tbl_14': tbl_14, 'tbl_15': tbl_15, 'tbl_16': tbl_16, 'tbl_17': tbl_17, 'tbl_18': tbl_18, 'tbl_19': tbl_19, 'tbl_20': tbl_20, 'tbl_21': tbl_21, 'tbl_22': tbl_22, 'tbl_23': tbl_23, 'tbl_24': tbl_24, 'tbl_25': tbl_25, 'tbl_26': tbl_26, 'tbl_27': tbl_27, 'tbl_28': tbl_28, 'tbl_29': tbl_29, 'tbl_30': tbl_30, 'tbl_31': tbl_31, 'tbl_32': tbl_32, 'tbl_33': tbl_33, 'tbl_34': tbl_34, 'tbl_35': tbl_35, 'tbl_36': tbl_36, 'tbl_37': tbl_37, 'tbl_38': tbl_38, 'tbl_39': tbl_39, 'W_top1': W_top1, 'b_top1': b_top1, 'W_top2': W_top2, 'b_top2': b_top2, 'W_top3': W_top3, 'L0_rec_bilinear_matrices': _L0_rec_in['bilinear_matrices']}

def reference(dense_ctx, ids, tbl_0, tbl_1, tbl_2, tbl_3, tbl_4, tbl_5, tbl_6, tbl_7, tbl_8, tbl_9, tbl_10, tbl_11, tbl_12, tbl_13, tbl_14, tbl_15, tbl_16, tbl_17, tbl_18, tbl_19, tbl_20, tbl_21, tbl_22, tbl_23, tbl_24, tbl_25, tbl_26, tbl_27, tbl_28, tbl_29, tbl_30, tbl_31, tbl_32, tbl_33, tbl_34, tbl_35, tbl_36, tbl_37, tbl_38, tbl_39, W_top1, b_top1, W_top2, b_top2, W_top3, L0_rec_bilinear_matrices):
    import jax
    import jax.numpy as jnp

    def _L0_rec_ref(inputs, bilinear_matrices):
        import jax, jax.numpy as jnp
        import numpy as np
        NUM_FIELDS = 40
        EMBED_DIM = 32
        BATCH = 512
        NUM_PAIRS = NUM_FIELDS * (NUM_FIELDS - 1) // 2
        num_fields = inputs.shape[1]
        iidx, jidx = jnp.triu_indices(num_fields, k=1)
        xi = inputs[:, iidx, :]
        xj = inputs[:, jidx, :]
        out = jnp.einsum('bpd,pde,bpe->bp', xi, bilinear_matrices, xj)
        return out
    e = jnp.stack([tbl_0[ids[:, 0]], tbl_1[ids[:, 1]], tbl_2[ids[:, 2]], tbl_3[ids[:, 3]], tbl_4[ids[:, 4]], tbl_5[ids[:, 5]], tbl_6[ids[:, 6]], tbl_7[ids[:, 7]], tbl_8[ids[:, 8]], tbl_9[ids[:, 9]], tbl_10[ids[:, 10]], tbl_11[ids[:, 11]], tbl_12[ids[:, 12]], tbl_13[ids[:, 13]], tbl_14[ids[:, 14]], tbl_15[ids[:, 15]], tbl_16[ids[:, 16]], tbl_17[ids[:, 17]], tbl_18[ids[:, 18]], tbl_19[ids[:, 19]], tbl_20[ids[:, 20]], tbl_21[ids[:, 21]], tbl_22[ids[:, 22]], tbl_23[ids[:, 23]], tbl_24[ids[:, 24]], tbl_25[ids[:, 25]], tbl_26[ids[:, 26]], tbl_27[ids[:, 27]], tbl_28[ids[:, 28]], tbl_29[ids[:, 29]], tbl_30[ids[:, 30]], tbl_31[ids[:, 31]], tbl_32[ids[:, 32]], tbl_33[ids[:, 33]], tbl_34[ids[:, 34]], tbl_35[ids[:, 35]], tbl_36[ids[:, 36]], tbl_37[ids[:, 37]], tbl_38[ids[:, 38]], tbl_39[ids[:, 39]]], axis=1)
    z = _L0_rec_ref(e, L0_rec_bilinear_matrices)
    z = z.reshape(z.shape[0], -1)
    h = jnp.concatenate([z, dense_ctx], axis=1)
    h = jnp.maximum(h @ W_top1 + b_top1, 0.0)
    h = jnp.maximum(h @ W_top2 + b_top2, 0.0)
    y = h @ W_top3
    return y

_drawn_inputs = setup_inputs


def setup_inputs(seed=0):
    import zlib

    import numpy as np

    out = dict(_drawn_inputs(seed))
    spreads = {'b_top1': (0.0, 0.1), 'b_top2': (0.0, 0.1)}
    factors = {'tbl_0': 3.523,
     'tbl_1': 3.296,
     'tbl_2': 3.39,
     'tbl_3': 2.961,
     'tbl_4': 3.248,
     'tbl_5': 3.002,
     'tbl_6': 3.388,
     'tbl_7': 3.264,
     'tbl_8': 3.118,
     'tbl_9': 2.999,
     'tbl_10': 3.266,
     'tbl_11': 3.539,
     'tbl_12': 3.04,
     'tbl_13': 3.287,
     'tbl_14': 3.173,
     'tbl_15': 3.406,
     'tbl_16': 3.178,
     'tbl_17': 3.125,
     'tbl_18': 3.519,
     'tbl_19': 3.349,
     'tbl_20': 3.12,
     'tbl_21': 3.326,
     'tbl_22': 3.273,
     'tbl_23': 3.024,
     'tbl_24': 3.395,
     'tbl_25': 3.437,
     'tbl_26': 3.175,
     'tbl_27': 3.374,
     'tbl_28': 3.236,
     'tbl_29': 3.235,
     'tbl_30': 3.187,
     'tbl_31': 2.984,
     'tbl_32': 3.305,
     'tbl_33': 3.318,
     'tbl_34': 3.321,
     'tbl_35': 3.104,
     'tbl_36': 3.52,
     'tbl_37': 3.415,
     'tbl_38': 3.388,
     'tbl_39': 3.098}
    for name, (base, spread) in spreads.items():
        noise = np.random.default_rng([zlib.crc32(name.encode()), seed]).standard_normal(out[name].shape)
        drawn = base * np.exp(spread * noise) if base else spread * noise
        out[name] = jnp.asarray(drawn.astype(out[name].dtype))
    for name, factor in factors.items():
        out[name] = (out[name] * factor).astype(out[name].dtype)
    return out
```

```python
from contextlib import ExitStack

import numpy as np

import concourse.bass as bass
from concourse import mybir

P = 128
BATCH = 2048
FIELDS = 40
EMB = 32
DENSE = 16
HID1 = 512
HID2 = 256
CHUNK = 256
BT = CHUNK // P
CHUNKS = BATCH // CHUNK
PER = P // EMB
BLOCKS = FIELDS // PER
BCOLS = BT * P

GROUPS = [(I, J) for J in range(BLOCKS) for I in range(J + 1)]
NG = len(GROUPS)
FIRST = [J * (J + 1) // 2 for J in range(BLOCKS)]


def members(g):
    I, J = GROUPS[g]
    return range(PER if I < J else PER - 1)


TILES = [(g, a) for g in range(NG) for a in members(g)]
TILE_OF = {ga: t for t, ga in enumerate(TILES)}
NT = len(TILES)
PIECE = 15
PIECES = NT // PIECE
ZK = 8
ZT = (NG + ZK - 1) // ZK
H1T = HID1 // P
H2T = HID2 // P

E_RING = 5
USES = BLOCKS // E_RING
ROWS_PER_BLOCK = PER * BT
FULL = 16
LEAD = 2

ALU = mybir.AluOpType
ACT = mybir.ActivationFunctionType
F32 = mybir.dt.float32
F32R = mybir.dt.float32r
I32 = mybir.dt.int32

assert NT == PIECE * PIECES and NG % ZK == ZK - 1 and DENSE == 4 * PER and CHUNKS % 2 == 0


def pieces_for(J):
    last = TILE_OF[(FIRST[J] + J, members(FIRST[J] + J)[-1])]
    return last // PIECE + 1


def turn_step(J):
    return max(FIRST[J] - LEAD, spread_step(J - 1)) if J else 0


def spread_step(J):
    return min(FIRST[J] + 1, FIRST[J] + J)


def build_tower(nc, t_ids, tables, t_m, t_w1, t_w2, t_cols, t_dense, t_ident, t_pick, t_spread, t_out):
    with ExitStack() as ctx:
        def sb(name, shape, dt=F32):
            return ctx.enter_context(nc.sbuf_tensor(name, shape, dt))

        def sem(name):
            return ctx.enter_context(nc.semaphore(name))

        W = sb("W", [P, NT * P], F32R)
        S = sb("S", [P, FIELDS, CHUNK], F32R)
        X = sb("X", [P, BLOCKS, CHUNK])
        E = sb("E", [P, E_RING, BT, PER * EMB])
        Hd = sb("Hd", [P, 2, CHUNK], F32R)
        Tl = sb("Tl", [P, 2, CHUNK], F32R)
        prod = sb("prod", [P, 2, PER, CHUNK])
        z = sb("z", [P, ZT, CHUNK])
        stage = sb("stage", [P, ZT * HID1 + H1T * HID2])
        cols = sb("cols", [P, H1T + 2 * H2T])
        dense = sb("dense", [P, CHUNK])
        idx = [sb(f"idx{p}", [P, BT * FIELDS], I32) for p in range(2)]
        ident = sb("ident", [P, P])
        pick = sb("pick", [P, 2 * EMB - PER])
        spread = sb("spread", [P, PER, 5 * EMB], F32R)
        y = sb("y", [1, CHUNK])

        b1, b2, w3 = cols[:, 0:H1T], cols[:, H1T:H1T + H2T], cols[:, H1T + H2T:]
        w1 = stage[:, 0:ZT * HID1].rearrange("p (t h) -> p t h", t=ZT)
        w2 = stage[:, ZT * HID1:].rearrange("p (t h) -> p t h", t=H1T)
        raw = [stage[:, s * PIECE * P:(s + 1) * PIECE * P] for s in range(2)]
        h1 = prod[:, 0, :, :]
        h2 = prod[:, 1, 0:H2T, :]
        spread_raw = prod[:, 0, :, 0:5 * EMB]
        assert H1T == PER and CHUNK >= 5 * EMB

        t_ps = ctx.enter_context(nc.psum_tensor("t_ps", [P, 2, PER, CHUNK], F32))
        turn_ps = ctx.enter_context(nc.psum_tensor("turn_ps", [P, 2, 2 * CHUNK], F32))
        out_ps = ctx.enter_context(nc.psum_tensor("out_ps", [P, 2, 2 * CHUNK], F32))
        z_ps = mlp_ps = out_ps[:, :, 0:CHUNK]

        consts_in = sem("consts_in")
        mlp_in = sem("mlp_in")
        raw_in = [sem(f"raw_in{s}") for s in range(2)]
        idx_in = [sem(f"idx_in{p}") for p in range(2)]
        dense_in = sem("dense_in")
        gathered = [sem(f"gathered{s}") for s in range(E_RING)]
        slot_taken = sem("slot_taken")
        y_out = sem("y_out")
        spread_ready = sem("spread_ready")
        heads_split = sem("heads_split")
        weights_split = sem("weights_split")
        turned = sem("turned")
        spread_done = sem("spread_done")
        turn_free = sem("turn_free")
        tails = sem("tails")
        t_ready = sem("t_ready")
        mul_done = sem("mul_done")
        summed = sem("summed")
        z_kept = sem("z_kept")
        z_last = sem("z_last")
        mlp_ready = sem("mlp_ready")
        mlp_kept = sem("mlp_kept")

        MLP_ITEMS = H1T + H2T + 1
        block = ctx.enter_context(nc.Block())

        @block.sync
        def _(sp):
            def load_ids(c, par):
                sp.dma_start(idx[par][:, :], t_ids[c]).then_inc(idx_in[par], FULL)

            def load_piece(n):
                s = n % 2
                if n >= 2:
                    sp.wait_ge(weights_split, n - 1)
                for q in range(PER):
                    sp.dma_start(raw[s][q * EMB:(q + 1) * EMB, :],
                                 t_m[:, n * PIECE * P:(n + 1) * PIECE * P]).then_inc(raw_in[s], FULL)

            def load_dense(c):
                sp.dma_start(dense[:, :], t_dense[c]).then_inc(dense_in, FULL)

            def store_y(c):
                sp.wait_ge(mlp_kept, (c + 1) * MLP_ITEMS)
                sp.dma_start(t_out[c], y[:, :]).then_inc(y_out, FULL)

            load_ids(0, 0)
            sp.dma_start(ident[:, :], t_ident).then_inc(consts_in, FULL)
            sp.dma_start(spread_raw, t_spread).then_inc(consts_in, FULL)
            load_piece(0)
            load_piece(1)
            load_ids(1, 1)
            sp.dma_start(pick[:, :], t_pick).then_inc(consts_in, FULL)
            sp.dma_start(cols[:, :], t_cols).then_inc(consts_in, FULL)
            load_dense(0)
            for n in range(2, PIECES):
                load_piece(n)
            sp.wait_ge(weights_split, PIECES)
            sp.dma_start(w1, t_w1.rearrange("(t p) h -> p t h", p=P)).then_inc(mlp_in, FULL)
            sp.dma_start(w2, t_w2.rearrange("(t p) h -> p t h", p=P)).then_inc(mlp_in, FULL)
            with sp.Fori(0, CHUNKS // 2 - 1) as pair:
                for par in range(2):
                    c = 2 * pair + par
                    sp.wait_ge(turned, (c + 1) * BLOCKS)
                    load_ids(c + 2, par)
                    sp.wait_ge(z_last, c + 1)
                    load_dense(c + 1)
                    store_y(c)
            sp.wait_ge(z_last, CHUNKS - 1)
            load_dense(CHUNKS - 1)
            store_y(CHUNKS - 2)
            store_y(CHUNKS - 1)
            sp.wait_ge(y_out, CHUNKS * FULL)

        @block.gpsimd
        def _(pool):
            def gather_chunk(c, par, first):
                for J in range(BLOCKS):
                    if not first or J >= E_RING:
                        pool.wait_ge(turned, c * BLOCKS + J - E_RING + 1)
                        pool.sem_inc(slot_taken, 1)
                    for bt in range(BT):
                        for s in range(PER):
                            f = J * PER + s
                            pool.indirect_dma_start(
                                out=E[:, J % E_RING, bt, s * EMB:(s + 1) * EMB], out_offset=None,
                                in_=tables[f],
                                in_offset=bass.IndirectOffsetOnAxis(
                                    ap=idx[par][:, bt * FIELDS + f:bt * FIELDS + f + 1], axis=0),
                            ).then_inc(gathered[J % E_RING], FULL)

            for par in range(2):
                pool.wait_ge(idx_in[par], FULL)
                gather_chunk(par, par, par == 0)
            with pool.Fori(1, CHUNKS // 2) as pair:
                for par in range(2):
                    pool.wait_ge(idx_in[par], (pair + 1) * FULL)
                    pool.sem_inc(slot_taken, 1)
                    gather_chunk(2 * pair + par, par, False)

        @block.tensor
        def _(pe):
            def turn(c, J, first):
                pe.wait_ge(gathered[J % E_RING], (c * USES + J // E_RING + 1) * ROWS_PER_BLOCK * FULL)
                n = 3 * J
                if not first or n >= 2:
                    pe.wait_ge(turn_free, c * 3 * BLOCKS + n - 1)
                for bt in range(BT):
                    last = pe.transpose(turn_ps[:, n % 2, bt * P:(bt + 1) * P], E[:, J % E_RING, bt, :], ident[:, :])
                last.then_inc(turned, 1)

            def spread_block(c, J):
                pe.wait_ge(tails, c * BLOCKS + J + 1)
                for pair in range(PER // 2):
                    n = 3 * J + 1 + pair
                    pe.wait_ge(turn_free, c * 3 * BLOCKS + n - 1)
                    for s in range(2 * pair, 2 * pair + 2):
                        out = turn_ps[:, n % 2, (s % 2) * CHUNK:(s % 2 + 1) * CHUNK]
                        pe.matmul(out, spread[:, s, 0:P], Hd[:, J % 2, :], start=True, stop=False)
                        last = pe.matmul(out, spread[:, s, EMB:EMB + P], Tl[:, J % 2, :], start=False, stop=True)
                    last.then_inc(spread_done, 1)

            def transform(c, g, first):
                I, J = GROUPS[g]
                if g >= 2:
                    pe.wait_ge(mul_done, c * NG + g - 1)
                if I == J:
                    pe.wait_ge(turn_free, c * 3 * BLOCKS + 3 * J + 3)
                if first:
                    pe.wait_ge(weights_split, TILE_OF[(g, members(g)[-1])] // PIECE + 1)
                for a in members(g):
                    t = TILE_OF[(g, a)]
                    last = pe.matmul(t_ps[:, g % 2, a, :], W[:, t * P:(t + 1) * P], S[:, PER * I + a, :],
                                     start=True, stop=True)
                last.then_inc(t_ready, 1)

            def sum_pairs(c, g, first):
                T, k = g // ZK, g % ZK
                pe.wait_ge(mul_done, c * NG + g + 1)
                if k == 0 and T >= 2:
                    pe.wait_ge(z_kept, c * (ZT - 1) + T - 1)
                if g == 0 and not first:
                    pe.wait_ge(mlp_kept, c * MLP_ITEMS)
                for a in members(g):
                    peers = [h for h in range(T * ZK, min((T + 1) * ZK, NG)) if a in members(h)]
                    last = pe.matmul(z_ps[a * EMB:(a + 1) * EMB, T % 2, :],
                                     pick[:, EMB - PER - PER * k:2 * EMB - PER - PER * k],
                                     prod[:, g % 2, a, :], start=(g == peers[0]), stop=(g == peers[-1]))
                last.then_inc(summed, 1)

            def mlp(c, first):
                def ready_to_write(n):
                    if n >= 2:
                        pe.wait_ge(mlp_kept, c * MLP_ITEMS + n - 1)
                pe.wait_ge(z_kept, (c + 1) * (ZT - 1))
                pe.wait_ge(z_last, c + 1)
                if first:
                    pe.wait_ge(mlp_in, 2 * FULL)
                for m in range(H1T):
                    ready_to_write(m)
                    for T in range(ZT):
                        last = pe.matmul(mlp_ps[:, m % 2, :], w1[:, T, m * P:(m + 1) * P], z[:, T, :],
                                         start=(T == 0), stop=(T == ZT - 1))
                    last.then_inc(mlp_ready, 1)
                pe.wait_ge(mlp_kept, c * MLP_ITEMS + H1T)
                for m in range(H2T):
                    for t in range(H1T):
                        last = pe.matmul(mlp_ps[:, (H1T + m) % 2, :], w2[:, t, m * P:(m + 1) * P], h1[:, t, :],
                                         start=(t == 0), stop=(t == H1T - 1))
                    last.then_inc(mlp_ready, 1)
                pe.wait_ge(mlp_kept, c * MLP_ITEMS + H1T + H2T)
                for t in range(H2T):
                    last = pe.matmul(mlp_ps[0:1, (H1T + H2T) % 2, :], w3[:, t:t + 1], h2[:, t, :],
                                     start=(t == 0), stop=(t == H2T - 1))
                last.then_inc(mlp_ready, 1)

            def chunk(c, first):
                for step in range(NG + 2):
                    for J in range(BLOCKS):
                        if turn_step(J) == step:
                            turn(c, J, first)
                        if spread_step(J) == step:
                            spread_block(c, J)
                    if step < NG:
                        transform(c, step, first)
                    if step >= 2:
                        sum_pairs(c, step - 2, first)
                mlp(c, first)

            pe.wait_ge(consts_in, 4 * FULL)
            pe.wait_ge(spread_ready, 1)
            chunk(0, True)
            with pe.Fori(1, CHUNKS) as c:
                chunk(c, False)

        @block.scalar
        def _(act):
            def split_heads(n):
                s = n % 2
                act.wait_ge(raw_in[s], (n // 2 + 1) * PER * FULL)
                nc.scalar.activation(W[:, n * PIECE * P:(n + 1) * PIECE * P], raw[s], ACT.Copy).then_inc(heads_split, 1)

            def keep_turned(c, J):
                src = turn_ps[:, (3 * J) % 2, 0:CHUNK]
                act.wait_ge(turned, c * BLOCKS + J + 1)
                nc.scalar.activation(X[:, J, :], src, ACT.Copy)
                nc.scalar.activation(Hd[:, J % 2, :], src, ACT.Copy).then_inc(turn_free, 1)

            def keep_spread(c, J):
                for pair in range(PER // 2):
                    act.wait_ge(spread_done, c * 2 * BLOCKS + 2 * J + pair + 1)
                    f = J * PER + 2 * pair
                    nc.scalar.activation(S[:, f:f + 2, :], turn_ps[:, (3 * J + 1 + pair) % 2, :].rearrange(
                        "p (f b) -> p f b", f=2), ACT.Copy).then_inc(turn_free, 1)

            def keep_z(c, T):
                act.wait_ge(summed, c * NG + (T + 1) * ZK)
                nc.scalar.activation(z[:, T, :], z_ps[:, T % 2, :], ACT.Copy).then_inc(z_kept, 1)

            def keep_mlp(c, first):
                for n in range(MLP_ITEMS):
                    act.wait_ge(mlp_ready, c * MLP_ITEMS + n + 1)
                    src = mlp_ps[:, n % 2, :]
                    if n < H1T:
                        out = nc.scalar.activation(h1[:, n, :], src, ACT.Relu, bias=b1[:, n:n + 1])
                    elif n < H1T + H2T:
                        m = n - H1T
                        out = nc.scalar.activation(h2[:, m, :], src, ACT.Relu, bias=b2[:, m:m + 1])
                    else:
                        if not first:
                            act.wait_ge(y_out, c * FULL)
                        out = nc.scalar.activation(y[:, :], mlp_ps[0:1, n % 2, :], ACT.Copy)
                    out.then_inc(mlp_kept, 1)

            def chunk(c, first):
                for step in range(NG + 2):
                    for J in range(BLOCKS):
                        if turn_step(J) == step:
                            keep_turned(c, J)
                            if first and J + 1 < BLOCKS:
                                for n in range(pieces_for(J), pieces_for(J + 1)):
                                    split_heads(n)
                        if spread_step(J) == step:
                            keep_spread(c, J)
                    if step >= 2 and (step - 2) % ZK == ZK - 1:
                        keep_z(c, (step - 2) // ZK)
                keep_mlp(c, first)

            act.wait_ge(consts_in, 4 * FULL)
            nc.scalar.activation(spread[:, :, :], spread_raw, ACT.Copy).then_inc(spread_ready, 1)
            for n in range(pieces_for(0)):
                split_heads(n)
            chunk(0, True)
            with act.Fori(1, CHUNKS) as c:
                chunk(c, False)

        @block.vector
        def _(dve):
            def split_tails(n):
                part = slice(n * PIECE * P, (n + 1) * PIECE * P)
                dve.wait_ge(heads_split, n + 1)
                nc.vector.tensor_tensor(W[P // 2:P, part], raw[n % 2][P // 2:P, :], W[P // 2:P, part].bitcast(F32),
                                        ALU.subtract).then_inc(weights_split, 1)

            def take_tails(c, J):
                dve.wait_ge(turn_free, c * 3 * BLOCKS + 3 * J + 1)
                nc.vector.tensor_tensor(Tl[:, J % 2, :], X[:, J, :], Hd[:, J % 2, :].bitcast(F32),
                                        ALU.subtract).then_inc(tails, 1)

            def multiply(c, g):
                J, n = GROUPS[g][1], len(members(g))
                dve.wait_ge(t_ready, c * NG + g + 1)
                if g >= 2:
                    dve.wait_ge(summed, c * NG + g - 1)
                nc.vector.tensor_tensor(prod[:, g % 2, 0:n, :], t_ps[:, g % 2, 0:n, :],
                                        X[:, J, :].unsqueeze(1).broadcast_to([P, n, CHUNK]),
                                        ALU.mult).then_inc(mul_done, 1)

            def chunk(c, first):
                for g in range(NG):
                    J = GROUPS[g][1]
                    if g == FIRST[J]:
                        take_tails(c, J)
                        if first and J + 1 < BLOCKS:
                            for n in range(pieces_for(J), pieces_for(J + 1)):
                                split_tails(n)
                    multiply(c, g)
                dve.wait_ge(summed, (c + 1) * NG)
                dve.wait_ge(dense_in, (c + 1) * FULL)
                nc.vector.tensor_tensor(z[:, ZT - 1, :], z_ps[:, (ZT - 1) % 2, :], dense[:, :],
                                        ALU.add).then_inc(z_last, 1)

            for n in range(pieces_for(0)):
                split_tails(n)
            chunk(0, True)
            with dve.Fori(1, CHUNKS) as c:
                chunk(c, False)


def pair_index(i, j):
    return i * FIELDS - i * (i + 1) // 2 + j - i - 1


def laid_out(inputs):
    ids = np.asarray(inputs["ids"]).reshape(CHUNKS, BT, P, FIELDS).transpose(0, 2, 1, 3)
    arrays = {"ids": np.ascontiguousarray(ids.reshape(CHUNKS, P, BT * FIELDS))}
    for f in range(FIELDS):
        arrays[f"tbl_{f}"] = np.ascontiguousarray(inputs[f"tbl_{f}"])
    M = np.asarray(inputs["L0_rec_bilinear_matrices"])
    W1 = np.asarray(inputs["W_top1"])
    pairs = FIELDS * (FIELDS - 1) // 2
    m = np.zeros((EMB, NT, PER, EMB), M.dtype)
    w1 = np.zeros((ZT * P, HID1), W1.dtype)
    for t, (g, a) in enumerate(TILES):
        I, J = GROUPS[g]
        for s in range(PER):
            i, j = PER * I + a, PER * J + s
            if i < j:
                m[:, t, s, :] = M[pair_index(i, j)]
                w1[g // ZK * P + EMB * a + PER * (g % ZK) + s] = W1[pair_index(i, j)]
    x = np.asarray(inputs["dense_ctx"])
    dense = np.zeros((CHUNKS, P, CHUNK), x.dtype)
    for r in range(DENSE):
        row = EMB * (r // PER) + PER * (NG % ZK) + r % PER
        w1[(ZT - 1) * P + row] = W1[pairs + r]
        dense[:, row, :] = x[:, r].reshape(CHUNKS, CHUNK)
    arrays["m"] = m.reshape(EMB, NT * P)
    arrays["w1"] = w1
    arrays["dense"] = dense
    arrays["w2"] = np.ascontiguousarray(inputs["W_top2"])
    arrays["cols"] = np.concatenate([np.asarray(inputs[key]).reshape(-1, P) for key in ("b_top1", "b_top2", "W_top3")]).T.copy()
    arrays["ident"] = np.eye(P, dtype=np.float32)
    pick = np.zeros((P, 2 * EMB - PER), np.float32)
    spread = np.zeros((P, PER, 5 * EMB), np.float32)
    for r in range(P):
        pick[r, EMB - PER + r // EMB] = 1
        for q in (0, 2, 4):
            spread[r, r // EMB, q * EMB + r % EMB] = 1
    arrays["pick"] = pick
    arrays["spread"] = spread
    return arrays


def kernel(**inputs):
    import concourse.bacc as bacc
    from concourse.bass_utils import run_bass_kernel_spmd

    nc = bacc.Bacc("TRN2", target_bir_lowering=False, num_devices=1)
    arrays = laid_out(inputs)
    ap = {name: nc.dram_tensor(f"in_{name}", a.shape, mybir.dt.from_np(a.dtype), kind="ExternalInput").ap()
          for name, a in arrays.items()}
    out = nc.dram_tensor("out_y", (CHUNKS, 1, CHUNK), F32, kind="ExternalOutput").ap()
    build_tower(nc, ap["ids"], [ap[f"tbl_{f}"] for f in range(FIELDS)], ap["m"], ap["w1"], ap["w2"],
                ap["cols"], ap["dense"], ap["ident"], ap["pick"], ap["spread"], out)
    result = run_bass_kernel_spmd(nc, [{f"in_{name}": a for name, a in arrays.items()}], core_ids=[0])
    return np.asarray(result.results[0]["out_y"]).reshape(BATCH, 1)
```

```python
from contextlib import ExitStack

import numpy as np

import concourse.bass as bass
from concourse import mybir

P = 128
BATCH = 2048
FIELDS = 40
EMB = 32
DENSE = 16
HID1 = 512
HID2 = 256
CHUNK = 256
BT = CHUNK // P
CHUNKS = BATCH // CHUNK
PER = P // EMB
BLOCKS = FIELDS // PER
BCOLS = BT * P

GROUPS = [(I, J) for J in range(BLOCKS) for I in range(J + 1)]
NG = len(GROUPS)
FIRST = [J * (J + 1) // 2 for J in range(BLOCKS)]


def members(g):
    I, J = GROUPS[g]
    return range(PER if I < J else PER - 1)


PAIRS = [(PER * I + a, PER * J + s) for g, (I, J) in enumerate(GROUPS) for a in members(g) for s in range(PER)
         if PER * I + a < PER * J + s]
PLACE = {pair: n for n, pair in enumerate(PAIRS)}
WCOLS = (1 + len(PAIRS)) * EMB
PIECE = 60
PIECES = len(PAIRS) // PIECE
RAW = PIECE * EMB
ZK = 8
ZT = (NG + ZK - 1) // ZK
H1T = HID1 // P
H2T = HID2 // P

E_RING = 5
USES = BLOCKS // E_RING
ROWS_PER_BLOCK = PER * BT
FULL = 16
LEAD = 2
PROD_RING = 3

ALU = mybir.AluOpType
ACT = mybir.ActivationFunctionType
F32 = mybir.dt.float32
F32R = mybir.dt.float32r
I32 = mybir.dt.int32

assert len(PAIRS) == PIECE * PIECES and NG % ZK == ZK - 1 and DENSE == 4 * PER and CHUNKS % 2 == 0


def tile_end(g, a):
    I, J = GROUPS[g]
    return (PLACE[PER * I + a, PER * J + PER - 1] + 2) * EMB


def pieces_of_tile(g, a):
    return (tile_end(g, a) - EMB - 1) // RAW + 1


def pieces_for(J):
    g = FIRST[J] + J
    return pieces_of_tile(g, members(g)[-1])


def spread_step(J, half):
    return FIRST[J] + min(1 + half, J)


def turn_step(J):
    return max(FIRST[J] - LEAD, spread_step(J - 1, 1)) if J else 0


def tails_group(J):
    return max(FIRST[J] - 1, 0)


MLP_ITEMS = H1T + H2T + 1
MLP_DEPTH = [ZT] * H1T + [H1T] * H2T + [H2T]
MLP_UNITS = [(n, k) for n in range(MLP_ITEMS) for k in range(MLP_DEPTH[n])]
KEEP_FIRST = 2 * ZK
MLP_AT = {("turn", 0): 4, ("spread", 0, 0): 2, ("spread", 0, 1): 2, ("turn", 1): 2, ("spread", 1, 1): 2, ("turn", 2): 2}
for step in range(2, NG):
    MLP_AT["step", step] = min(1, len(MLP_UNITS) - sum(MLP_AT.values()))


def points():
    for step in range(NG):
        for J in range(BLOCKS):
            if turn_step(J) == step:
                yield "turn", J
            for half in range(2):
                if spread_step(J, half) == step:
                    yield "spread", J, half
        yield "step", step


MLP_PART = {}
given = 0
for point in points():
    MLP_PART[point] = MLP_UNITS[given:given + MLP_AT.get(point, 0)]
    given += MLP_AT.get(point, 0)
assert given == len(MLP_UNITS)
assert all(n >= H1T for step in range(KEEP_FIRST, NG) for n, k in MLP_PART["step", step])


def build_tower(nc, t_ids, tables, t_m, t_w1, t_w2, t_cols, t_dense, t_ident, t_pick, t_spread, t_out):
    with ExitStack() as ctx:
        def sb(name, shape, dt=F32):
            return ctx.enter_context(nc.sbuf_tensor(name, shape, dt))

        def sem(name):
            return ctx.enter_context(nc.semaphore(name))

        W = sb("W", [P, WCOLS], F32R)
        S = sb("S", [P, FIELDS - 1, CHUNK], F32R)
        X = sb("X", [P, BLOCKS, CHUNK])
        E = sb("E", [P, E_RING, BT, PER * EMB])
        HL = sb("HL", [P, 2, 2, CHUNK], F32R)
        prod = sb("prod", [P, PROD_RING, PER, CHUNK])
        z = sb("z", [P, ZT, CHUNK])
        stage = sb("stage", [P, ZT * HID1 + H1T * HID2])
        cols = sb("cols", [P, H1T + 2 * H2T])
        dense = sb("dense", [P, CHUNK])
        idx = [sb(f"idx{p}", [P, BT * FIELDS], I32) for p in range(2)]
        ident = sb("ident", [P, P])
        pick = sb("pick", [P, 2 * EMB - PER])
        spread = sb("spread", [P, PER, P], F32R)
        h1 = sb("h1", [P, H1T, CHUNK])
        h2 = sb("h2", [P, H2T, CHUNK])
        y = sb("y", [1, CHUNK])

        b1, b2, w3 = cols[:, 0:H1T], cols[:, H1T:H1T + H2T], cols[:, H1T + H2T:]
        w1 = stage[:, 0:ZT * HID1].rearrange("p (t h) -> p t h", t=ZT)
        w2 = stage[:, ZT * HID1:].rearrange("p (t h) -> p t h", t=H1T)
        raw = [stage[:, s * RAW:(s + 1) * RAW] for s in range(2)]
        spread_raw = prod[:, 0, :, 0:P]

        t_ps = ctx.enter_context(nc.psum_tensor("t_ps", [P, 2, PER, CHUNK], F32))
        turn_ps = ctx.enter_context(nc.psum_tensor("turn_ps", [P, 2 * CHUNK], F32))
        z_ps = ctx.enter_context(nc.psum_tensor("z_ps", [P, 2, 2 * CHUNK], F32))
        mlp_ps = ctx.enter_context(nc.psum_tensor("mlp_ps", [P, 2 * CHUNK], F32))

        consts_in = sem("consts_in")
        mlp_in = sem("mlp_in")
        raw_in = [sem(f"raw_in{s}") for s in range(2)]
        idx_in = [sem(f"idx_in{p}") for p in range(2)]
        dense_in = sem("dense_in")
        gathered = [sem(f"gathered{s}") for s in range(E_RING)]
        slot_taken = sem("slot_taken")
        y_out = sem("y_out")
        y_free = sem("y_free")
        spread_ready = sem("spread_ready")
        heads_split = sem("heads_split")
        weights_split = sem("weights_split")
        turned = sem("turned")
        spread_done = sem("spread_done")
        turn_free = sem("turn_free")
        tails = sem("tails")
        t_ready = sem("t_ready")
        mul_done = sem("mul_done")
        summed = sem("summed")
        z_kept = sem("z_kept")
        z_last = sem("z_last")
        mlp_ready = sem("mlp_ready")
        mlp_kept = sem("mlp_kept")

        block = ctx.enter_context(nc.Block())

        @block.sync
        def _(sp):
            def load_ids(c, par):
                sp.dma_start(idx[par][:, :], t_ids[c]).then_inc(idx_in[par], FULL)

            def load_piece(n):
                s = n % 2
                if n >= 2:
                    sp.wait_ge(weights_split, n - 1)
                for q in range(PER):
                    sp.dma_start(raw[s][q * EMB:(q + 1) * EMB, :],
                                 t_m[:, n * RAW:(n + 1) * RAW]).then_inc(raw_in[s], FULL)

            def load_dense(c):
                sp.dma_start(dense[:, :], t_dense[c]).then_inc(dense_in, FULL)

            def store_y(c):
                sp.wait_ge(mlp_kept, (c + 1) * MLP_ITEMS)
                sp.dma_start(t_out[c], y[:, :]).then_inc(y_out, FULL)
                sp.wait_ge(y_out, (c + 1) * FULL)
                sp.sem_inc(y_free, 1)

            load_ids(0, 0)
            sp.sem_inc(y_free, 1)
            sp.dma_start(ident[:, :], t_ident).then_inc(consts_in, FULL)
            sp.dma_start(spread_raw, t_spread).then_inc(consts_in, FULL)
            load_piece(0)
            load_piece(1)
            load_ids(1, 1)
            sp.dma_start(pick[:, :], t_pick).then_inc(consts_in, FULL)
            sp.dma_start(cols[:, :], t_cols).then_inc(consts_in, FULL)
            load_dense(0)
            for n in range(2, PIECES):
                load_piece(n)
            sp.wait_ge(weights_split, PIECES)
            sp.dma_start(w1, t_w1.rearrange("(t p) h -> p t h", p=P)).then_inc(mlp_in, FULL)
            sp.dma_start(w2, t_w2.rearrange("(t p) h -> p t h", p=P)).then_inc(mlp_in, FULL)
            with sp.Fori(0, CHUNKS // 2 - 1) as pair:
                for par in range(2):
                    c = 2 * pair + par
                    sp.wait_ge(turned, (c + 1) * BLOCKS)
                    load_ids(c + 2, par)
                    sp.wait_ge(z_last, c + 1)
                    load_dense(c + 1)
                    store_y(c)
            sp.wait_ge(z_last, CHUNKS - 1)
            load_dense(CHUNKS - 1)
            store_y(CHUNKS - 2)
            store_y(CHUNKS - 1)
            sp.wait_ge(y_out, CHUNKS * FULL)

        @block.gpsimd
        def _(pool):
            def gather_chunk(c, par, first):
                for J in range(BLOCKS):
                    if not first or J >= E_RING:
                        pool.wait_ge(turned, c * BLOCKS + J - E_RING + 1)
                        pool.sem_inc(slot_taken, 1)
                    for bt in range(BT):
                        for s in range(PER):
                            f = J * PER + s
                            pool.indirect_dma_start(
                                out=E[:, J % E_RING, bt, s * EMB:(s + 1) * EMB], out_offset=None,
                                in_=tables[f],
                                in_offset=bass.IndirectOffsetOnAxis(
                                    ap=idx[par][:, bt * FIELDS + f:bt * FIELDS + f + 1], axis=0),
                            ).then_inc(gathered[J % E_RING], FULL)

            for par in range(2):
                pool.wait_ge(idx_in[par], FULL)
                gather_chunk(par, par, par == 0)
            with pool.Fori(1, CHUNKS // 2) as pair:
                for par in range(2):
                    pool.wait_ge(idx_in[par], (pair + 1) * FULL)
                    pool.sem_inc(slot_taken, 1)
                    gather_chunk(2 * pair + par, par, False)

        @block.tensor
        def _(pe):
            def turn(c, J, first):
                pe.wait_ge(gathered[J % E_RING], (c * USES + J // E_RING + 1) * ROWS_PER_BLOCK * FULL)
                if not first or J > 0:
                    pe.wait_ge(turn_free, c * 3 * BLOCKS + 3 * J)
                for bt in range(BT):
                    last = pe.transpose(turn_ps[:, bt * P:(bt + 1) * P], E[:, J % E_RING, bt, :], ident[:, :])
                last.then_inc(turned, 1)

            def spread_half(c, J, half):
                if half == 0:
                    pe.wait_ge(tails, c * BLOCKS + J + 1)
                pe.wait_ge(turn_free, c * 3 * BLOCKS + 3 * J + 1 + half)
                for n in range(2):
                    last = pe.matmul(turn_ps[:, n * CHUNK:(n + 1) * CHUNK], spread[:, 2 * half + n, :],
                                     HL[:, J % 2, half, :], start=True, stop=True)
                last.then_inc(spread_done, 1)

            def transform(c, g, first):
                I, J = GROUPS[g]
                if g >= 2:
                    pe.wait_ge(mul_done, c * NG + g - 1)
                if I == J:
                    pe.wait_ge(turn_free, c * 3 * BLOCKS + 3 * J + 3)
                if first:
                    pe.wait_ge(weights_split, pieces_of_tile(g, members(g)[-1]))
                for a in members(g):
                    end = tile_end(g, a)
                    last = pe.matmul(t_ps[:, g % 2, a, :], W[:, end - P:end], S[:, PER * I + a, :],
                                     start=True, stop=True)
                last.then_inc(t_ready, 1)

            def sum_pairs(c, g):
                T, k = g // ZK, g % ZK
                pe.wait_ge(mul_done, c * NG + g + 1)
                if k == 0 and T >= 2:
                    pe.wait_ge(z_kept, c * (ZT - 1) + T - 1)
                for a in members(g):
                    peers = [h for h in range(T * ZK, min((T + 1) * ZK, NG)) if a in members(h)]
                    last = pe.matmul(z_ps[a * EMB:(a + 1) * EMB, T % 2, 0:CHUNK],
                                     pick[:, EMB - PER - PER * k:2 * EMB - PER - PER * k],
                                     prod[:, g % PROD_RING, a, :], start=(g == peers[0]), stop=(g == peers[-1]))
                last.then_inc(summed, 1)

            def mlp_matmul(done, n, k):
                if n == 0 and k == 0:
                    pe.wait_ge(mlp_in, 2 * FULL)
                    pe.wait_ge(z_kept, done * (ZT - 1))
                if n == 0 and k == ZT - 1:
                    pe.wait_ge(z_last, done)
                if n > 0 and k == 0:
                    pe.wait_ge(mlp_kept, (done - 1) * MLP_ITEMS + n)
                if n < H1T:
                    out, weights, x = mlp_ps[:, 0:CHUNK], w1[:, k, n * P:(n + 1) * P], z[:, k, :]
                elif n < H1T + H2T:
                    m = n - H1T
                    out, weights, x = mlp_ps[:, 0:CHUNK], w2[:, k, m * P:(m + 1) * P], h1[:, k, :]
                else:
                    out, weights, x = mlp_ps[0:1, 0:CHUNK], w3[:, k:k + 1], h2[:, k, :]
                last = pe.matmul(out, weights, x, start=(k == 0), stop=(k == MLP_DEPTH[n] - 1))
                if k == MLP_DEPTH[n] - 1:
                    last.then_inc(mlp_ready, 1)

            def mlp_after(c, first, *point):
                if not first:
                    for n, k in MLP_PART[point]:
                        mlp_matmul(c, n, k)

            def chunk(c, first):
                for step in range(NG + 2):
                    for J in range(BLOCKS):
                        if turn_step(J) == step:
                            turn(c, J, first)
                            mlp_after(c, first, "turn", J)
                        for half in range(2):
                            if spread_step(J, half) == step:
                                spread_half(c, J, half)
                                mlp_after(c, first, "spread", J, half)
                    if step < NG:
                        transform(c, step, first)
                    if step >= 2:
                        sum_pairs(c, step - 2)
                    if step < NG:
                        mlp_after(c, first, "step", step)

            pe.wait_ge(consts_in, 4 * FULL)
            pe.wait_ge(spread_ready, 1)
            chunk(0, True)
            with pe.Fori(1, CHUNKS) as c:
                chunk(c, False)
            for n, k in MLP_UNITS:
                mlp_matmul(CHUNKS, n, k)

        @block.scalar
        def _(act):
            def split_heads(n):
                s = n % 2
                act.wait_ge(raw_in[s], (n // 2 + 1) * PER * FULL)
                nc.scalar.activation(W[:, EMB + n * RAW:EMB + (n + 1) * RAW], raw[s], ACT.Copy).then_inc(heads_split, 1)

            def keep_turned(c, J):
                src = turn_ps[:, 0:CHUNK]
                act.wait_ge(turned, c * BLOCKS + J + 1)
                nc.scalar.activation(X[:, J, :], src, ACT.Copy)
                nc.scalar.activation(HL[0:P // 2, J % 2, 0, :], src[0:P // 2, :], ACT.Copy)
                nc.scalar.activation(HL[P // 2:P, J % 2, 1, :], src[P // 2:P, :], ACT.Copy).then_inc(turn_free, 1)

            def keep_spread(c, J, half):
                f = J * PER + 2 * half
                kept = min(f + 2, FIELDS - 1) - f
                act.wait_ge(spread_done, c * 2 * BLOCKS + 2 * J + half + 1)
                nc.scalar.activation(S[:, f:f + kept, :], turn_ps[:, 0:kept * CHUNK].rearrange(
                    "p (f b) -> p f b", f=kept), ACT.Copy).then_inc(turn_free, 1)

            def keep_z(c, T):
                act.wait_ge(summed, c * NG + (T + 1) * ZK)
                nc.scalar.activation(z[:, T, :], z_ps[:, T % 2, 0:CHUNK], ACT.Copy).then_inc(z_kept, 1)

            def keep_mlp(done, n):
                act.wait_ge(mlp_ready, (done - 1) * MLP_ITEMS + n + 1)
                if n < H1T:
                    out = nc.scalar.activation(h1[:, n, :], mlp_ps[:, 0:CHUNK], ACT.Relu, bias=b1[:, n:n + 1])
                elif n < H1T + H2T:
                    m = n - H1T
                    out = nc.scalar.activation(h2[:, m, :], mlp_ps[:, 0:CHUNK], ACT.Relu, bias=b2[:, m:m + 1])
                else:
                    act.wait_ge(y_free, done)
                    out = nc.scalar.activation(y[:, :], mlp_ps[0:1, 0:CHUNK], ACT.Copy)
                out.then_inc(mlp_kept, 1)

            def keep_mlp_after(c, first, *point):
                if not first:
                    for n, k in MLP_PART[point]:
                        if k == MLP_DEPTH[n] - 1:
                            keep_mlp(c, n)

            def chunk(c, first):
                for step in range(NG + 2):
                    for J in range(BLOCKS):
                        if turn_step(J) == step:
                            keep_turned(c, J)
                            keep_mlp_after(c, first, "turn", J)
                            if first and J + 1 < BLOCKS:
                                for n in range(pieces_for(J), pieces_for(J + 1)):
                                    split_heads(n)
                        for half in range(2):
                            if spread_step(J, half) == step:
                                keep_spread(c, J, half)
                                keep_mlp_after(c, first, "spread", J, half)
                    if step >= 2 and (step - 2) % ZK == ZK - 1 and step - 2 >= ZK:
                        keep_z(c, (step - 2) // ZK)
                    if step == KEEP_FIRST:
                        keep_z(c, 0)
                    if step < NG:
                        keep_mlp_after(c, first, "step", step)

            act.wait_ge(consts_in, 4 * FULL)
            nc.scalar.activation(spread[:, :, :], spread_raw, ACT.Copy).then_inc(spread_ready, 1)
            for n in range(pieces_for(0)):
                split_heads(n)
            chunk(0, True)
            with act.Fori(1, CHUNKS) as c:
                chunk(c, False)
            for n in range(MLP_ITEMS):
                keep_mlp(CHUNKS, n)

        @block.vector
        def _(dve):
            def split_tails(n):
                part = slice(EMB + n * RAW, EMB + (n + 1) * RAW)
                dve.wait_ge(heads_split, n + 1)
                nc.vector.tensor_tensor(W[P // 2:P, part], raw[n % 2][P // 2:P, :], W[P // 2:P, part].bitcast(F32),
                                        ALU.subtract).then_inc(weights_split, 1)

            def take_tails(c, J):
                dve.wait_ge(turn_free, c * 3 * BLOCKS + 3 * J + 1)
                low, high = slice(0, P // 2), slice(P // 2, P)
                nc.vector.tensor_tensor(HL[high, J % 2, 0, :], X[low, J, :], HL[low, J % 2, 0, :].bitcast(F32),
                                        ALU.subtract)
                nc.vector.tensor_tensor(HL[low, J % 2, 1, :], X[high, J, :], HL[high, J % 2, 1, :].bitcast(F32),
                                        ALU.subtract).then_inc(tails, 1)

            def multiply(c, g):
                J, n = GROUPS[g][1], len(members(g))
                dve.wait_ge(t_ready, c * NG + g + 1)
                if g >= PROD_RING:
                    dve.wait_ge(summed, c * NG + g - PROD_RING + 1)
                nc.vector.tensor_tensor(prod[:, g % PROD_RING, 0:n, :], t_ps[:, g % 2, 0:n, :],
                                        X[:, J, :].unsqueeze(1).broadcast_to([P, n, CHUNK]),
                                        ALU.mult).then_inc(mul_done, 1)

            def chunk(c, first):
                for g in range(NG):
                    for J in range(BLOCKS):
                        if tails_group(J) == g:
                            take_tails(c, J)
                            if first and J + 1 < BLOCKS:
                                for n in range(pieces_for(J), pieces_for(J + 1)):
                                    split_tails(n)
                    multiply(c, g)
                dve.wait_ge(summed, (c + 1) * NG)
                dve.wait_ge(dense_in, (c + 1) * FULL)
                nc.vector.tensor_tensor(z[:, ZT - 1, :], z_ps[:, (ZT - 1) % 2, 0:CHUNK], dense[:, :],
                                        ALU.add).then_inc(z_last, 1)

            nc.vector.memset(W[:, 0:EMB].bitcast(F32), 0.0)
            for n in range(pieces_for(0)):
                split_tails(n)
            chunk(0, True)
            with dve.Fori(1, CHUNKS) as c:
                chunk(c, False)


def pair_index(i, j):
    return i * FIELDS - i * (i + 1) // 2 + j - i - 1


def laid_out(inputs):
    ids = np.asarray(inputs["ids"]).reshape(CHUNKS, BT, P, FIELDS).transpose(0, 2, 1, 3)
    arrays = {"ids": np.ascontiguousarray(ids.reshape(CHUNKS, P, BT * FIELDS))}
    for f in range(FIELDS):
        arrays[f"tbl_{f}"] = np.ascontiguousarray(inputs[f"tbl_{f}"])
    M = np.asarray(inputs["L0_rec_bilinear_matrices"])
    W1 = np.asarray(inputs["W_top1"])
    pairs = FIELDS * (FIELDS - 1) // 2
    m = np.stack([M[pair_index(i, j)] for i, j in PAIRS], axis=1)
    w1 = np.zeros((ZT * P, HID1), W1.dtype)
    for g, (I, J) in enumerate(GROUPS):
        for a in members(g):
            for s in range(PER):
                if PER * I + a < PER * J + s:
                    w1[g // ZK * P + EMB * a + PER * (g % ZK) + s] = W1[pair_index(PER * I + a, PER * J + s)]
    x = np.asarray(inputs["dense_ctx"])
    dense = np.zeros((CHUNKS, P, CHUNK), x.dtype)
    for r in range(DENSE):
        row = EMB * (r // PER) + PER * (NG % ZK) + r % PER
        w1[(ZT - 1) * P + row] = W1[pairs + r]
        dense[:, row, :] = x[:, r].reshape(CHUNKS, CHUNK)
    arrays["m"] = m.reshape(EMB, len(PAIRS) * EMB)
    arrays["w1"] = w1
    arrays["dense"] = dense
    arrays["w2"] = np.ascontiguousarray(inputs["W_top2"])
    arrays["cols"] = np.concatenate([np.asarray(inputs[key]).reshape(-1, P) for key in ("b_top1", "b_top2", "W_top3")]).T.copy()
    arrays["ident"] = np.eye(P, dtype=np.float32)
    pick = np.zeros((P, 2 * EMB - PER), np.float32)
    spread = np.zeros((P, PER, P), np.float32)
    for r in range(P):
        pick[r, EMB - PER + r // EMB] = 1
        quadrant, row = divmod(r, EMB)
        for s in range(PER):
            if quadrant % 2 == s % 2:
                head = (quadrant < 2) == (s < 2)
                for q in (0, 2) if head else (1, 3):
                    spread[r, s, q * EMB + row] = 1
    arrays["pick"] = pick
    arrays["spread"] = spread
    return arrays


def kernel(**inputs):
    import concourse.bacc as bacc
    from concourse.bass_utils import run_bass_kernel_spmd

    nc = bacc.Bacc("TRN2", target_bir_lowering=False, num_devices=1)
    arrays = laid_out(inputs)
    ap = {name: nc.dram_tensor(f"in_{name}", a.shape, mybir.dt.from_np(a.dtype), kind="ExternalInput").ap()
          for name, a in arrays.items()}
    out = nc.dram_tensor("out_y", (CHUNKS, 1, CHUNK), F32, kind="ExternalOutput").ap()
    build_tower(nc, ap["ids"], [ap[f"tbl_{f}"] for f in range(FIELDS)], ap["m"], ap["w1"], ap["w2"],
                ap["cols"], ap["dense"], ap["ident"], ap["pick"], ap["spread"], out)
    result = run_bass_kernel_spmd(nc, [{f"in_{name}": a for name, a in arrays.items()}], core_ids=[0])
    return np.asarray(result.results[0]["out_y"]).reshape(BATCH, 1)
```

```python
from contextlib import ExitStack

import numpy as np

import concourse.bass as bass
from concourse import mybir

P = 128
BATCH = 2048
FIELDS = 40
EMB = 32
DENSE = 16
HID1 = 512
HID2 = 256
CHUNK = 256
BT = CHUNK // P
CHUNKS = BATCH // CHUNK
PER = P // EMB
BLOCKS = FIELDS // PER

GROUPS = [(I, J) for J in range(BLOCKS) for I in range(J + 1)]
NG = len(GROUPS)
FIRST = [J * (J + 1) // 2 for J in range(BLOCKS)]


def members(g):
    I, J = GROUPS[g]
    return range(PER if I < J else PER - 1)


PAIRS = [(PER * I + a, PER * J + s) for g, (I, J) in enumerate(GROUPS) for a in members(g) for s in range(PER)
         if PER * I + a < PER * J + s]
PLACE = {pair: n for n, pair in enumerate(PAIRS)}
WCOLS = (1 + len(PAIRS)) * EMB
PIECE = 30
PIECES = len(PAIRS) // PIECE
RAW = PIECE * EMB
RAW_RING = 4
ZK = 8
ZT = (NG + ZK - 1) // ZK
H1T = HID1 // P
H2T = HID2 // P

E_RING = 5
USES = BLOCKS // E_RING
ROWS_PER_BLOCK = PER * BT
FULL = 16
LEAD = 2
PROD_RING = 4
X_RING = 3
X_SLOT = [J % X_RING for J in range(BLOCKS - 2)] + [0, 2]

ALU = mybir.AluOpType
ACT = mybir.ActivationFunctionType
F32 = mybir.dt.float32
F32R = mybir.dt.float32r
I32 = mybir.dt.int32

assert len(PAIRS) == PIECE * PIECES and NG % 2 and NG % ZK == ZK - 1 and DENSE == 4 * PER and CHUNKS % 2 == 0


def tile_end(g, a):
    I, J = GROUPS[g]
    return (PLACE[PER * I + a, PER * J + PER - 1] + 2) * EMB


def pieces_of_tile(g, a):
    return (tile_end(g, a) - EMB - 1) // RAW + 1


SPLIT_FIRST, SPLIT_TURNED, SPLIT_SPREAD = 4, 2, 4
SPLIT_AFTER = [0] * NG
for g, pieces in ((0, 2), (1, 2), (3, 2), (4, 2), (6, 1), (7, 1), (8, 1), (11, 1), (12, 1), (17, 1)):
    SPLIT_AFTER[g] = pieces
SPLIT_START = SPLIT_FIRST + SPLIT_TURNED + SPLIT_SPREAD
for g in range(22, NG, 2):
    SPLIT_AFTER[g] = min(1, PIECES - SPLIT_START - sum(SPLIT_AFTER))
SPLIT_BY = [SPLIT_START + sum(SPLIT_AFTER[:g]) for g in range(NG)]
assert all(SPLIT_BY[g] >= pieces_of_tile(g, members(g)[-1]) for g in range(NG))
assert SPLIT_BY[-1] + SPLIT_AFTER[-1] == PIECES


def spread_step(J, half):
    return FIRST[J] + min(1 + half, J)


def turn_step(J):
    return max(FIRST[J] - LEAD, spread_step(J - 1, 1) if J > 1 else 0)


def tails_group(J):
    return max(FIRST[J] - 1, 0)


NEXT_TURN = spread_step(BLOCKS - 1, 1) + 1
NEXT_SPREAD = [NEXT_TURN + 2, NEXT_TURN + 3]
NEXT_TAILS = NEXT_TURN + 1
assert NEXT_SPREAD[1] < NG

Z_TWICE = 3


def z_place(T, par):
    return T + Z_TWICE * par if T < Z_TWICE else T + Z_TWICE


def keep_step(T):
    return (T + 1) * ZK + 2


MLP_ITEMS = H1T + H2T + 1
MLP_DEPTH = [ZT] * H1T + [H1T] * H2T + [H2T]
MLP_UNITS = [(n, k) for n in range(MLP_ITEMS) for k in range(MLP_DEPTH[n])]


def points():
    for step in range(NG):
        for J in range(1, BLOCKS):
            if turn_step(J) == step:
                yield "turn", J
            for half in range(2):
                if spread_step(J, half) == step:
                    yield "spread", J, half
        yield "step", step


def dealt(at, units):
    part, given = {}, 0
    for point in points():
        part[point] = units[given:given + at.get(point, 0)]
        given += at.get(point, 0)
    assert given == len(units)
    return part


def filled(at, total, steps):
    at = dict(at)
    for step in steps:
        at["step", step] = min(1, total - sum(at.values()))
    return at


MLP_PART = dealt(filled({("turn", 1): 2, ("spread", 1, 0): 2, ("spread", 1, 1): 2, ("turn", 2): 2,
                         ("spread", 2, 0): 1, ("spread", 2, 1): 1, ("turn", 3): 1, ("spread", 3, 0): 1, ("spread", 3, 1): 1},
                        len(MLP_UNITS), range(3, NG, 2)), MLP_UNITS)

LAST_PART = dealt(filled({("turn", 1): 3, ("spread", 1, 0): 3, ("spread", 1, 1): 2, ("turn", 2): 2, ("spread", 2, 0): 1,
                          ("spread", 2, 1): 1, ("turn", 3): 2, ("spread", 3, 0): 2, ("spread", 3, 1): 2, ("turn", 4): 2},
                         len(MLP_UNITS), range(1, NG, 2)), MLP_UNITS)
OWN_FROM = keep_step(Z_TWICE) + 3
EARLY = [(n, k) for k in range(ZT - 2) for n in range(2)]
EARLY_PART = dealt(filled({}, len(EARLY), [*range(OWN_FROM, NG, 2), NG - 1]), EARLY)
LATE = [(n, k) for k in range(ZT - 1) for n in range(H1T) if (n, k) not in EARLY]
for part in MLP_PART, LAST_PART:
    assert all(n >= H1T for step in range(keep_step(Z_TWICE), NG) for n, k in part["step", step])
assert not any(LAST_PART["step", step] for step in range(OWN_FROM, NG))


def build_tower(nc, t_ids, tables, t_m, t_w1, t_w2, t_cols, t_dense, t_ident, t_pick, t_spread, t_out):
    with ExitStack() as ctx:
        def sb(name, shape, dt=F32):
            return ctx.enter_context(nc.sbuf_tensor(name, shape, dt))

        def sem(name):
            return ctx.enter_context(nc.semaphore(name))

        W = sb("W", [P, WCOLS], F32R)
        S = sb("S", [P, FIELDS - 1, CHUNK], F32R)
        X = sb("X", [P, X_RING, CHUNK])
        E = sb("E", [P, E_RING, BT, PER * EMB])
        HL = sb("HL", [P, 2, 2, CHUNK], F32R)
        prod = sb("prod", [P, PROD_RING, PER, CHUNK])
        z = sb("z", [P, ZT + Z_TWICE, CHUNK])
        stage = sb("stage", [P, ZT * HID1 + H1T * HID2])
        cols = sb("cols", [P, H1T + 2 * H2T])
        dense = sb("dense", [P, CHUNK])
        idx = [sb(f"idx{p}", [P, BT * FIELDS], I32) for p in range(2)]
        ident = sb("ident", [P, P])
        pick = sb("pick", [P, 2 * EMB - PER])
        spread = sb("spread", [P, PER, P], F32R)
        h1 = sb("h1", [P, H1T, CHUNK])
        h2 = sb("h2", [P, H2T, CHUNK])
        y = sb("y", [1, CHUNK])

        b1, b2, w3 = cols[:, 0:H1T], cols[:, H1T:H1T + H2T], cols[:, H1T + H2T:]
        w1 = stage[:, 0:ZT * HID1].rearrange("p (t h) -> p t h", t=ZT)
        w2 = stage[:, ZT * HID1:].rearrange("p (t h) -> p t h", t=H1T)
        raw = [stage[:, s * RAW:(s + 1) * RAW] for s in range(RAW_RING)]
        assert RAW_RING * RAW <= ZT * HID1 + H1T * HID2
        spread_raw = prod[:, 0, :, 0:P]

        t_ps = ctx.enter_context(nc.psum_tensor("t_ps", [P, 2, PER, CHUNK], F32))
        turn_ps = ctx.enter_context(nc.psum_tensor("turn_ps", [P, 2 * CHUNK], F32))
        z_ps = ctx.enter_context(nc.psum_tensor("z_ps", [P, 2, 2 * CHUNK], F32))
        mlp_ps = ctx.enter_context(nc.psum_tensor("mlp_ps", [P, 2 * CHUNK], F32))

        consts_in = sem("consts_in")
        mlp_in = sem("mlp_in")
        raw_in = [sem(f"raw_in{s}") for s in range(RAW_RING)]
        idx_in = [sem(f"idx_in{p}") for p in range(2)]
        dense_in = sem("dense_in")
        gathered = [sem(f"gathered{s}") for s in range(E_RING)]
        slot_taken = sem("slot_taken")
        y_out = sem("y_out")
        y_free = sem("y_free")
        spread_ready = sem("spread_ready")
        heads_split = sem("heads_split")
        weights_split = sem("weights_split")
        turned = sem("turned")
        spread_done = sem("spread_done")
        turn_free = sem("turn_free")
        tails = sem("tails")
        t_ready = sem("t_ready")
        mul_done = sem("mul_done")
        summed = sem("summed")
        z_kept = sem("z_kept")
        z_last = sem("z_last")
        mlp_ready = sem("mlp_ready")
        mlp_kept = sem("mlp_kept")

        block = ctx.enter_context(nc.Block())

        @block.sync
        def _(sp):
            def load_ids(c, par):
                sp.dma_start(idx[par][:, :], t_ids[c]).then_inc(idx_in[par], FULL)

            def load_piece(n):
                s = n % RAW_RING
                if n >= RAW_RING:
                    sp.wait_ge(weights_split, n - RAW_RING + 1)
                sp.dma_start(raw[s], t_m[:, n * RAW:(n + 1) * RAW]).then_inc(raw_in[s], FULL)

            def load_dense(c):
                sp.dma_start(dense[:, :], t_dense[c]).then_inc(dense_in, FULL)

            def store_y(c):
                sp.wait_ge(mlp_kept, (c + 1) * MLP_ITEMS)
                sp.dma_start(t_out[c], y[:, :]).then_inc(y_out, FULL)
                sp.wait_ge(y_out, (c + 1) * FULL)
                sp.sem_inc(y_free, 1)

            load_ids(0, 0)
            sp.dma_start(spread_raw, t_spread).then_inc(consts_in, FULL)
            sp.dma_start(ident[:, :], t_ident).then_inc(consts_in, FULL)
            sp.dma_start(pick[:, :], t_pick).then_inc(consts_in, FULL)
            sp.dma_start(cols[:, :], t_cols).then_inc(consts_in, FULL)
            sp.sem_inc(y_free, 1)
            for n in range(RAW_RING):
                load_piece(n)
            load_ids(1, 1)
            load_dense(0)
            for n in range(RAW_RING, PIECES):
                load_piece(n)
            sp.wait_ge(weights_split, PIECES)
            sp.dma_start(w1, t_w1.rearrange("(t p) h -> p t h", p=P)).then_inc(mlp_in, FULL)
            sp.dma_start(w2, t_w2.rearrange("(t p) h -> p t h", p=P)).then_inc(mlp_in, FULL)
            with sp.Fori(0, CHUNKS // 2 - 1) as pair:
                for par in range(2):
                    c = 2 * pair + par
                    sp.wait_ge(turned, (c + 1) * BLOCKS)
                    load_ids(c + 2, par)
                    sp.wait_ge(z_last, c + 1)
                    load_dense(c + 1)
                    store_y(c)
            sp.wait_ge(z_last, CHUNKS - 1)
            load_dense(CHUNKS - 1)
            store_y(CHUNKS - 2)
            store_y(CHUNKS - 1)
            sp.wait_ge(y_out, CHUNKS * FULL)

        @block.gpsimd
        def _(pool):
            def gather_chunk(c, par, first):
                for J in range(BLOCKS):
                    if not first or J >= E_RING:
                        pool.wait_ge(turned, c * BLOCKS + J - E_RING + 1)
                        pool.sem_inc(slot_taken, 1)
                    for bt in range(BT):
                        for s in range(PER):
                            f = J * PER + s
                            pool.indirect_dma_start(
                                out=E[:, J % E_RING, bt, s * EMB:(s + 1) * EMB], out_offset=None,
                                in_=tables[f],
                                in_offset=bass.IndirectOffsetOnAxis(
                                    ap=idx[par][:, bt * FIELDS + f:bt * FIELDS + f + 1], axis=0),
                            ).then_inc(gathered[J % E_RING], FULL)

            for par in range(2):
                pool.wait_ge(idx_in[par], FULL)
                gather_chunk(par, par, par == 0)
            with pool.Fori(1, CHUNKS // 2) as pair:
                for par in range(2):
                    pool.wait_ge(idx_in[par], (pair + 1) * FULL)
                    pool.sem_inc(slot_taken, 1)
                    gather_chunk(2 * pair + par, par, False)

        @block.tensor
        def _(pe):
            def turn(c, J, first):
                pe.wait_ge(gathered[J % E_RING], (c * USES + J // E_RING + 1) * ROWS_PER_BLOCK * FULL)
                if not first:
                    pe.wait_ge(turn_free, c * 3 * BLOCKS + 3 * J)
                for bt in range(BT):
                    last = pe.transpose(turn_ps[:, bt * P:(bt + 1) * P], E[:, J % E_RING, bt, :], ident[:, :])
                last.then_inc(turned, 1)

            def spread_half(c, J, half):
                if half == 0:
                    pe.wait_ge(tails, c * BLOCKS + J + 1)
                pe.wait_ge(turn_free, c * 3 * BLOCKS + 3 * J + 1 + half)
                for n in range(2):
                    last = pe.matmul(turn_ps[:, n * CHUNK:(n + 1) * CHUNK], spread[:, 2 * half + n, :],
                                     HL[:, J % 2, half, :], start=True, stop=True)
                last.then_inc(spread_done, 1)

            def transform(c, g, first):
                I, J = GROUPS[g]
                if g >= 2:
                    pe.wait_ge(mul_done, c * NG + g - 1)
                if I == J:
                    pe.wait_ge(turn_free, c * 3 * BLOCKS + 3 * J + 3)
                if first:
                    pe.wait_ge(weights_split, pieces_of_tile(g, members(g)[-1]))
                for a in members(g):
                    end = tile_end(g, a)
                    last = pe.matmul(t_ps[:, g % 2, a, :], W[:, end - P:end], S[:, PER * I + a, :],
                                     start=True, stop=True)
                last.then_inc(t_ready, 1)

            def sum_pairs(c, g):
                T, k = g // ZK, g % ZK
                pe.wait_ge(mul_done, c * NG + g + 1)
                if k == 0 and T >= 2:
                    pe.wait_ge(z_kept, c * (ZT - 1) + T - 1)
                for a in members(g):
                    peers = [h for h in range(T * ZK, min((T + 1) * ZK, NG)) if a in members(h)]
                    last = pe.matmul(z_ps[a * EMB:(a + 1) * EMB, T % 2, 0:CHUNK],
                                     pick[:, EMB - PER - PER * k:2 * EMB - PER - PER * k],
                                     prod[:, g % PROD_RING, a, :], start=(g == peers[0]), stop=(g == peers[-1]))
                last.then_inc(summed, 1)

            def mlp_matmul(done, par, n, k):
                if n == 0 and k == 0:
                    pe.wait_ge(mlp_in, 2 * FULL)
                    pe.wait_ge(z_kept, done * (ZT - 1))
                if n == 0 and k == ZT - 1:
                    pe.wait_ge(z_last, done)
                if n > 0 and k == 0:
                    pe.wait_ge(mlp_kept, (done - 1) * MLP_ITEMS + n)
                if n < H1T:
                    out, weights, x = mlp_ps[:, 0:CHUNK], w1[:, k, n * P:(n + 1) * P], z[:, z_place(k, par), :]
                elif n < H1T + H2T:
                    m = n - H1T
                    out, weights, x = mlp_ps[:, 0:CHUNK], w2[:, k, m * P:(m + 1) * P], h1[:, k, :]
                else:
                    out, weights, x = mlp_ps[0:1, 0:CHUNK], w3[:, k:k + 1], h2[:, k, :]
                last = pe.matmul(out, weights, x, start=(k == 0), stop=(k == MLP_DEPTH[n] - 1))
                if k == MLP_DEPTH[n] - 1:
                    last.then_inc(mlp_ready, 1)

            def mlp_after(c, par, first, last, *point):
                if not first:
                    for n, k in (LAST_PART if last else MLP_PART)[point]:
                        mlp_matmul(c, 1 - par, n, k)

            def own_matmul(n, k):
                bank = mlp_ps if n < 2 else turn_ps
                if n % 2 == 0:
                    if k < ZT - 1:
                        pe.wait_ge(z_kept, (CHUNKS - 1) * (ZT - 1) + k + 1)
                    else:
                        pe.wait_ge(z_last, CHUNKS)
                last = pe.matmul(bank[:, n % 2 * CHUNK:(n % 2 + 1) * CHUNK], w1[:, k, n * P:(n + 1) * P],
                                 z[:, z_place(k, (CHUNKS - 1) % 2), :], start=(k == 0 and n % 2 == 0),
                                 stop=(k == ZT - 1), skip_group_check=True)
                if k == ZT - 1:
                    last.then_inc(mlp_ready, 1)

            def chunk(c, par, first=False, last=False):
                for step in range(NG + 2):
                    for J in range(1, BLOCKS):
                        if turn_step(J) == step:
                            turn(c, J, False)
                            mlp_after(c, par, first, last, "turn", J)
                        for half in range(2):
                            if spread_step(J, half) == step:
                                spread_half(c, J, half)
                                mlp_after(c, par, first, last, "spread", J, half)
                    if step == NEXT_TURN and not last:
                        turn(c + 1, 0, False)
                    for half in range(2):
                        if step == NEXT_SPREAD[half] and not last:
                            spread_half(c + 1, 0, half)
                    if step < NG:
                        transform(c, step, first)
                        mlp_after(c, par, first, last, "step", step)
                    if last and step == OWN_FROM:
                        pe.wait_ge(mlp_kept, c * MLP_ITEMS)
                    if last and step < NG:
                        for n, k in EARLY_PART["step", step]:
                            own_matmul(n, k)
                    if step % 2 == 0:
                        for g in (step - 3, step - 2):
                            if g >= 0:
                                sum_pairs(c, g)
                if not first and not last:
                    pe.wait_ge(mlp_kept, c * MLP_ITEMS)

            def last_mlp():
                pe.wait_ge(turn_free, CHUNKS * 3 * BLOCKS)
                for n, k in LATE + [(n, ZT - 1) for n in range(H1T)]:
                    own_matmul(n, k)
                for m in range(H2T):
                    for k in range(H1T):
                        if m == 0:
                            pe.wait_ge(mlp_kept, (CHUNKS - 1) * MLP_ITEMS + k + 1)
                        last = pe.matmul(t_ps[:, m, 0, :], w2[:, k, m * P:(m + 1) * P], h1[:, k, :],
                                         start=(k == 0), stop=(k == H1T - 1))
                    last.then_inc(mlp_ready, 1)
                for k in range(H2T):
                    pe.wait_ge(mlp_kept, (CHUNKS - 1) * MLP_ITEMS + H1T + k + 1)
                    last = pe.matmul(t_ps[0:1, 0, PER // 2, :], w3[:, k:k + 1], h2[:, k, :],
                                     start=(k == 0), stop=(k == H2T - 1))
                last.then_inc(mlp_ready, 1)

            pe.wait_ge(consts_in, 4 * FULL)
            pe.wait_ge(spread_ready, 1)
            turn(0, 0, True)
            for half in range(2):
                spread_half(0, 0, half)
            chunk(0, 0, first=True)
            with pe.Fori(0, CHUNKS // 2 - 1) as pair:
                chunk(2 * pair + 1, 1)
                chunk(2 * pair + 2, 0)
            chunk(CHUNKS - 1, 1, last=True)
            last_mlp()

        @block.scalar
        def _(act):
            def split_heads(n):
                s = n % RAW_RING
                act.wait_ge(raw_in[s], (n // RAW_RING + 1) * FULL)
                nc.scalar.activation(W[:, EMB + n * RAW:EMB + (n + 1) * RAW], raw[s], ACT.Copy).then_inc(heads_split, 1)

            def keep_turned(c, J):
                src = turn_ps[:, 0:CHUNK]
                act.wait_ge(turned, c * BLOCKS + J + 1)
                nc.scalar.activation(X[:, X_SLOT[J], :], src, ACT.Copy)
                nc.scalar.activation(HL[0:P // 2, J % 2, 0, :], src[0:P // 2, :], ACT.Copy)
                nc.scalar.activation(HL[P // 2:P, J % 2, 1, :], src[P // 2:P, :], ACT.Copy).then_inc(turn_free, 1)

            def keep_spread(c, J, half):
                f = J * PER + 2 * half
                kept = min(f + 2, FIELDS - 1) - f
                act.wait_ge(spread_done, c * 2 * BLOCKS + 2 * J + half + 1)
                nc.scalar.activation(S[:, f:f + kept, :], turn_ps[:, 0:kept * CHUNK].rearrange(
                    "p (f b) -> p f b", f=kept), ACT.Copy).then_inc(turn_free, 1)

            def keep_z(c, par, T):
                act.wait_ge(summed, c * NG + (T + 1) * ZK)
                nc.scalar.activation(z[:, z_place(T, par), :], z_ps[:, T % 2, 0:CHUNK], ACT.Copy).then_inc(z_kept, 1)

            def keep_mlp(done, n):
                act.wait_ge(mlp_ready, (done - 1) * MLP_ITEMS + n + 1)
                if n < H1T:
                    out = nc.scalar.activation(h1[:, n, :], mlp_ps[:, 0:CHUNK], ACT.Relu, bias=b1[:, n:n + 1])
                elif n < H1T + H2T:
                    m = n - H1T
                    out = nc.scalar.activation(h2[:, m, :], mlp_ps[:, 0:CHUNK], ACT.Relu, bias=b2[:, m:m + 1])
                else:
                    act.wait_ge(y_free, done)
                    out = nc.scalar.activation(y[:, :], mlp_ps[0:1, 0:CHUNK], ACT.Copy)
                out.then_inc(mlp_kept, 1)

            def keep_mlp_after(c, first, last, *point):
                if not first:
                    for n, k in (LAST_PART if last else MLP_PART)[point]:
                        if k == MLP_DEPTH[n] - 1:
                            keep_mlp(c, n)

            def keep_last_mlp():
                base = (CHUNKS - 1) * MLP_ITEMS
                for n in range(H1T):
                    act.wait_ge(mlp_ready, base + n // 2 * 2 + 2)
                    src = (mlp_ps if n < 2 else turn_ps)[:, n % 2 * CHUNK:(n % 2 + 1) * CHUNK]
                    nc.scalar.activation(h1[:, n, :], src, ACT.Relu, bias=b1[:, n:n + 1]).then_inc(mlp_kept, 1)
                for m in range(H2T):
                    act.wait_ge(mlp_ready, base + H1T + m + 1)
                    nc.scalar.activation(h2[:, m, :], t_ps[:, m, 0, :], ACT.Relu, bias=b2[:, m:m + 1]).then_inc(mlp_kept, 1)
                act.wait_ge(mlp_ready, base + MLP_ITEMS)
                act.wait_ge(y_free, CHUNKS)
                nc.scalar.activation(y[:, :], t_ps[0:1, 0, PER // 2, :], ACT.Copy).then_inc(mlp_kept, 1)

            def chunk(c, par, first=False, last=False):
                for step in range(NG + 2):
                    for J in range(1, BLOCKS):
                        if turn_step(J) == step:
                            keep_turned(c, J)
                            keep_mlp_after(c, first, last, "turn", J)
                        for half in range(2):
                            if spread_step(J, half) == step:
                                keep_spread(c, J, half)
                                keep_mlp_after(c, first, last, "spread", J, half)
                    if step == NEXT_TURN and not last:
                        keep_turned(c + 1, 0)
                    for half in range(2):
                        if step == NEXT_SPREAD[half] and not last:
                            keep_spread(c + 1, 0, half)
                    for T in range(ZT - 1):
                        if keep_step(T) == step:
                            keep_z(c, par, T)
                    if step < NG:
                        keep_mlp_after(c, first, last, "step", step)
                        if first:
                            for n in range(SPLIT_BY[step], SPLIT_BY[step] + SPLIT_AFTER[step]):
                                split_heads(n)

            act.wait_ge(consts_in, 4 * FULL)
            nc.scalar.activation(spread[:, :, :], spread_raw, ACT.Copy).then_inc(spread_ready, 1)
            for n in range(SPLIT_FIRST):
                split_heads(n)
            keep_turned(0, 0)
            for n in range(SPLIT_FIRST, SPLIT_FIRST + SPLIT_TURNED):
                split_heads(n)
            for half in range(2):
                keep_spread(0, 0, half)
            for n in range(SPLIT_FIRST + SPLIT_TURNED, SPLIT_START):
                split_heads(n)
            chunk(0, 0, first=True)
            with act.Fori(0, CHUNKS // 2 - 1) as pair:
                chunk(2 * pair + 1, 1)
                chunk(2 * pair + 2, 0)
            chunk(CHUNKS - 1, 1, last=True)
            keep_last_mlp()

        @block.vector
        def _(dve):
            def split_tails(n):
                part = slice(EMB + n * RAW, EMB + (n + 1) * RAW)
                dve.wait_ge(heads_split, n + 1)
                nc.vector.tensor_tensor(W[P // 2:P, part], raw[n % RAW_RING][P // 2:P, :], W[P // 2:P, part].bitcast(F32),
                                        ALU.subtract).then_inc(weights_split, 1)

            def take_tails(c, J):
                dve.wait_ge(turn_free, c * 3 * BLOCKS + 3 * J + 1)
                low, high = slice(0, P // 2), slice(P // 2, P)
                nc.vector.tensor_tensor(HL[high, J % 2, 0, :], X[low, X_SLOT[J], :], HL[low, J % 2, 0, :].bitcast(F32),
                                        ALU.subtract)
                nc.vector.tensor_tensor(HL[low, J % 2, 1, :], X[high, X_SLOT[J], :], HL[high, J % 2, 1, :].bitcast(F32),
                                        ALU.subtract).then_inc(tails, 1)

            def multiply(c, g):
                J, n = GROUPS[g][1], len(members(g))
                dve.wait_ge(t_ready, c * NG + g + 1)
                if g >= PROD_RING:
                    dve.wait_ge(summed, c * NG + g - PROD_RING + 1)
                nc.vector.tensor_tensor(prod[:, g % PROD_RING, 0:n, :], t_ps[:, g % 2, 0:n, :],
                                        X[:, X_SLOT[J], :].unsqueeze(1).broadcast_to([P, n, CHUNK]),
                                        ALU.mult).then_inc(mul_done, 1)

            def chunk(c, par, first=False, last=False):
                for g in range(NG):
                    for J in range(1, BLOCKS):
                        if tails_group(J) == g:
                            take_tails(c, J)
                    if g == NEXT_TAILS and not last:
                        take_tails(c + 1, 0)
                    multiply(c, g)
                    if first:
                        for n in range(SPLIT_BY[g], SPLIT_BY[g] + SPLIT_AFTER[g]):
                            split_tails(n)
                dve.wait_ge(summed, (c + 1) * NG)
                dve.wait_ge(dense_in, (c + 1) * FULL)
                nc.vector.tensor_tensor(z[:, z_place(ZT - 1, par), :], z_ps[:, (ZT - 1) % 2, 0:CHUNK], dense[:, :],
                                        ALU.add).then_inc(z_last, 1)

            nc.vector.memset(W[:, 0:EMB].bitcast(F32), 0.0)
            for n in range(SPLIT_FIRST):
                split_tails(n)
            take_tails(0, 0)
            for n in range(SPLIT_FIRST, SPLIT_START):
                split_tails(n)
            chunk(0, 0, first=True)
            with dve.Fori(0, CHUNKS // 2 - 1) as pair:
                chunk(2 * pair + 1, 1)
                chunk(2 * pair + 2, 0)
            chunk(CHUNKS - 1, 1, last=True)


def pair_index(i, j):
    return i * FIELDS - i * (i + 1) // 2 + j - i - 1


def laid_out(inputs):
    ids = np.asarray(inputs["ids"]).reshape(CHUNKS, BT, P, FIELDS).transpose(0, 2, 1, 3)
    arrays = {"ids": np.ascontiguousarray(ids.reshape(CHUNKS, P, BT * FIELDS))}
    for f in range(FIELDS):
        arrays[f"tbl_{f}"] = np.ascontiguousarray(inputs[f"tbl_{f}"])
    M = np.asarray(inputs["L0_rec_bilinear_matrices"])
    W1 = np.asarray(inputs["W_top1"])
    pairs = FIELDS * (FIELDS - 1) // 2
    m = np.stack([M[pair_index(i, j)] for i, j in PAIRS], axis=1)
    w1 = np.zeros((ZT * P, HID1), W1.dtype)
    for g, (I, J) in enumerate(GROUPS):
        for a in members(g):
            for s in range(PER):
                if PER * I + a < PER * J + s:
                    w1[g // ZK * P + EMB * a + PER * (g % ZK) + s] = W1[pair_index(PER * I + a, PER * J + s)]
    x = np.asarray(inputs["dense_ctx"])
    dense = np.zeros((CHUNKS, P, CHUNK), x.dtype)
    for r in range(DENSE):
        row = EMB * (r // PER) + PER * (NG % ZK) + r % PER
        w1[(ZT - 1) * P + row] = W1[pairs + r]
        dense[:, row, :] = x[:, r].reshape(CHUNKS, CHUNK)
    arrays["m"] = np.concatenate([m.reshape(EMB, len(PAIRS) * EMB)] * PER)
    arrays["w1"] = w1
    arrays["dense"] = dense
    arrays["w2"] = np.ascontiguousarray(inputs["W_top2"])
    arrays["cols"] = np.concatenate([np.asarray(inputs[key]).reshape(-1, P) for key in ("b_top1", "b_top2", "W_top3")]).T.copy()
    arrays["ident"] = np.eye(P, dtype=np.float32)
    pick = np.zeros((P, 2 * EMB - PER), np.float32)
    spread = np.zeros((P, PER, P), np.float32)
    for r in range(P):
        pick[r, EMB - PER + r // EMB] = 1
        quadrant, row = divmod(r, EMB)
        for s in range(PER):
            if quadrant % 2 == s % 2:
                head = (quadrant < 2) == (s < 2)
                for q in (0, 2) if head else (1, 3):
                    spread[r, s, q * EMB + row] = 1
    arrays["pick"] = pick
    arrays["spread"] = spread
    return arrays


def kernel(**inputs):
    import concourse.bacc as bacc
    from concourse.bass_utils import run_bass_kernel_spmd

    nc = bacc.Bacc("TRN2", target_bir_lowering=False, num_devices=1)
    arrays = laid_out(inputs)
    ap = {name: nc.dram_tensor(f"in_{name}", a.shape, mybir.dt.from_np(a.dtype), kind="ExternalInput").ap()
          for name, a in arrays.items()}
    out = nc.dram_tensor("out_y", (CHUNKS, 1, CHUNK), F32, kind="ExternalOutput").ap()
    build_tower(nc, ap["ids"], [ap[f"tbl_{f}"] for f in range(FIELDS)], ap["m"], ap["w1"], ap["w2"],
                ap["cols"], ap["dense"], ap["ident"], ap["pick"], ap["spread"], out)
    result = run_bass_kernel_spmd(nc, [{f"in_{name}": a for name, a in arrays.items()}], core_ids=[0])
    return np.asarray(result.results[0]["out_y"]).reshape(BATCH, 1)
```
